# Optimizing a Trainium2 kernel written in Bass

```python
import numpy as np
import jax
import jax.numpy as jnp

def _softmax(x, axis=-1):
    return jax.nn.softmax(x, axis=axis)

def _gelu(x):
    return jax.nn.gelu(x, approximate=True)

def _silu(x):
    return jax.nn.silu(x)

def _sigmoid(x):
    return jax.nn.sigmoid(x)

def _layernorm(x, axis=-1, eps=1e-05):
    m = jnp.mean(x, axis=axis, keepdims=True)
    v = jnp.var(x, axis=axis, keepdims=True)
    return (x - m) / jnp.sqrt(v + eps)

def _scatter_add(tgt, idx, src, axis=0):
    return tgt.at[idx].add(src)

def _segment_sum(src, seg, n):
    return jax.ops.segment_sum(src, seg, n)
kernel_name = 'mk_flamingo_gated_d1_seqx_r8_5dbd93'

def setup_inputs(seed: int=0):
    np.random.seed(seed)
    _w = jnp.asarray

    def _rec_inputs():
        import jax
        import jax.numpy as jnp
        _rk = jax.random.key(seed)
        x = 0.0003765 + 1 * jax.random.normal(jax.random.fold_in(_rk, 1), (8, 128, 256), jnp.float32)
        _lenS = 128 - jax.random.randint(jax.random.fold_in(_rk, 7), (8,), 0, max(1, 128 // 4) + 1, jnp.int32)
        _lenS2 = 128 - jax.random.randint(jax.random.fold_in(_rk, 8), (8,), 0, max(1, 128 // 4) + 1, jnp.int32)
        _ctx_2048P = jax.random.normal(jax.random.fold_in(_rk, 11), (8, 16, 256), jnp.float32)
        _ctx_2048c = jax.random.dirichlet(jax.random.fold_in(_rk, 511), 0.3 * jnp.ones((16,), jnp.float32), (8, 128))
        _ctx_2048t = jnp.einsum('bsk,bkd->bsd', _ctx_2048c, _ctx_2048P)
        _ctx_2048t = _ctx_2048t * jax.lax.rsqrt(jnp.mean(jnp.square(_ctx_2048t)) + 1e-12) * 0.953939
        ctx_2048 = -0.000292821 + 1.00034 * (_ctx_2048t + 0.3 * jax.random.normal(jax.random.fold_in(_rk, 611), (8, 128, 256), jnp.float32))
        _g = jax.random.normal(jax.random.fold_in(_rk, 9001), (2, 1), jnp.float32)
        _g = jnp.sign(_g) * jnp.maximum(jnp.abs(_g), 1.0) + (_g == 0) * 1.0
        g_xattn = _g[0]
        g_ffn = _g[1]
        return (x, ctx_2048, g_xattn, g_ffn)
    x, ctx_2048, g_xattn, g_ffn = _rec_inputs()

    def _L0_xattn_setup():
        import jax, jax.numpy as jnp
        import numpy as np
        key = jax.random.key(seed)
        k1, k2, k3, k4, k5 = jax.random.split(key, 5)
        B, D_MODEL, L = (2, 128, 256)
        HEAD_DIM = 8
        H = D_MODEL // HEAD_DIM
        return {'k': jax.random.normal(k1, (B, D_MODEL, L), dtype=jnp.float32), 'v': jax.random.normal(k2, (B, D_MODEL, L), dtype=jnp.float32), 'q': jax.random.normal(k3, (B, D_MODEL, L), dtype=jnp.float32), 'ssm_kernel': jax.random.normal(k4, (H, L), dtype=jnp.float32), 'D': jax.random.normal(k5, (H,), dtype=jnp.float32), 'head_dim': HEAD_DIM}
    _L0_xattn_all = _L0_xattn_setup()
    _L0_xattn_in = {k: v for k, v in _L0_xattn_all.items() if k in ('ssm_kernel', 'D')}
    del _L0_xattn_all

    def _L0_ffn_setup():
        import jax, jax.numpy as jnp
        import numpy as np
        B, S, H = (2, 256, 256)
        E, K, F = (32, 4, 176)
        FS = 704
        EPS = 1e-06
        CAP = 128
        key = jax.random.key(seed)
        ks = jax.random.split(key, 10)
        s = 0.02
        return {'hidden_states': jax.random.normal(ks[0], (B, S, H), jnp.float32), 'w_norm': 1.0 + 0.02 * jax.random.normal(ks[1], (H,), jnp.float32), 'w_router': s * jax.random.normal(ks[2], (H, E), jnp.float32), 'w_gate': s * jax.random.normal(ks[3], (E, H, F), jnp.float32), 'w_up': s * jax.random.normal(ks[4], (E, H, F), jnp.float32), 'w_down': s * jax.random.normal(ks[5], (E, F, H), jnp.float32), 'sw_gate': s * jax.random.normal(ks[6], (H, FS), jnp.float32), 'sw_up': s * jax.random.normal(ks[7], (H, FS), jnp.float32), 'sw_down': s * jax.random.normal(ks[8], (FS, H), jnp.float32), 'w_shared_gate': s * jax.random.normal(ks[9], (H, 1), jnp.float32)}
    _L0_ffn_all = _L0_ffn_setup()
    _L0_ffn_in = {k: v for k, v in _L0_ffn_all.items() if k in ('w_norm', 'w_router', 'w_gate', 'w_up', 'w_down', 'sw_gate', 'sw_up', 'sw_down', 'w_shared_gate')}
    del _L0_ffn_all
    return {'x': x, 'ctx_2048': ctx_2048, 'g_xattn': g_xattn, 'g_ffn': g_ffn, 'L0_xattn_ssm_kernel': _L0_xattn_in['ssm_kernel'], 'L0_xattn_D': _L0_xattn_in['D'], 'L0_ffn_w_norm': _L0_ffn_in['w_norm'], 'L0_ffn_w_router': _L0_ffn_in['w_router'], 'L0_ffn_w_gate': _L0_ffn_in['w_gate'], 'L0_ffn_w_up': _L0_ffn_in['w_up'], 'L0_ffn_w_down': _L0_ffn_in['w_down'], 'L0_ffn_sw_gate': _L0_ffn_in['sw_gate'], 'L0_ffn_sw_up': _L0_ffn_in['sw_up'], 'L0_ffn_sw_down': _L0_ffn_in['sw_down'], 'L0_ffn_w_shared_gate': _L0_ffn_in['w_shared_gate']}

def reference(x, ctx_2048, g_xattn, g_ffn, L0_xattn_ssm_kernel, L0_xattn_D, L0_ffn_w_norm, L0_ffn_w_router, L0_ffn_w_gate, L0_ffn_w_up, L0_ffn_w_down, L0_ffn_sw_gate, L0_ffn_sw_up, L0_ffn_sw_down, L0_ffn_w_shared_gate):
    import jax
    import jax.numpy as jnp

    def _L0_xattn_ref(k, v, q, ssm_kernel, D, head_dim):
        import jax, jax.numpy as jnp
        import numpy as np
        B, HD, L = k.shape
        H = HD // head_dim
        fft_size = 2 * L
        k_ = k.reshape(B, H, head_dim, L)
        v_ = v.reshape(B, H, head_dim, L)
        q_ = q.reshape(B, H, head_dim, L)
        kv = jnp.einsum('bhil,bhjl->bijhl', k_, v_)
        kv_f = jnp.fft.rfft(kv, n=fft_size)
        kernel_f = jnp.fft.rfft(ssm_kernel, n=fft_size)
        y = jnp.fft.irfft(kv_f * kernel_f, n=fft_size)[..., :L]
        out = y + kv * D[None, None, None, :, None]
        out = jnp.einsum('bijhl,bhil->bjhl', out, q_)
        out = jnp.transpose(out, (0, 2, 1, 3)).reshape(B, H * head_dim, L)
        return out.astype(k.dtype)

    def _L0_ffn_ref(hidden_states, w_norm, w_router, w_gate, w_up, w_down, sw_gate, sw_up, sw_down, w_shared_gate):
        import jax, jax.numpy as jnp
        import numpy as np
        B, S, H = (2, 256, 256)
        E, K, F = (32, 4, 176)
        FS = 704
        EPS = 1e-06
        CAP = 128
        inp = hidden_states
        xf = inp.astype(jnp.float32)
        var = jnp.mean(xf * xf, axis=-1, keepdims=True)
        x = (w_norm * (xf * jax.lax.rsqrt(var + EPS))).astype(inp.dtype)
        Bq, Sq, Hq = x.shape
        x = x.reshape(-1, Hq)
        T = Bq * Sq
        logits = x @ w_router
        probs = jax.nn.softmax(logits.astype(jnp.float32), axis=-1)
        w_topk, sel = jax.lax.top_k(probs, K)
        w_topk = w_topk.astype(x.dtype)
        flat_e = sel.reshape(-1)
        order = jnp.argsort(flat_e)
        sorted_e = flat_e[order]
        counts = jnp.zeros((E,), jnp.int32).at[flat_e].add(1)
        starts = jnp.cumsum(counts) - counts
        pos = jnp.arange(T * K) - starts[sorted_e]
        tok = order // K
        valid = pos < CAP
        dest = jnp.where(valid, pos, CAP)
        buf = jnp.zeros((E, CAP + 1, Hq), x.dtype).at[sorted_e, dest].set(x[tok])
        buf = buf[:, :CAP]
        g = jnp.einsum('ech,ehf->ecf', buf, w_gate)
        u = jnp.einsum('ech,ehf->ecf', buf, w_up)
        y = jnp.einsum('ecf,efh->ech', jax.nn.silu(g) * u, w_down)
        wv = w_topk.reshape(-1)[order] * valid.astype(x.dtype)
        gath = y[sorted_e, jnp.minimum(pos, CAP - 1)]
        out = jnp.zeros((T, Hq), x.dtype).at[tok].add(gath * wv[:, None])
        sh = jax.nn.silu(x @ sw_gate) * (x @ sw_up) @ sw_down
        sh = jax.nn.sigmoid(x @ w_shared_gate) * sh
        out = out + sh
        return inp + out.reshape(Bq, Sq, Hq)
    x = x + jnp.tanh(g_xattn[0]) * _L0_xattn_ref(ctx_2048, ctx_2048, _layernorm(x, axis=-1), L0_xattn_ssm_kernel, L0_xattn_D, 8)
    x = x + jnp.tanh(g_ffn[0]) * _L0_ffn_ref(_layernorm(x, axis=-1), L0_ffn_w_norm, L0_ffn_w_router, L0_ffn_w_gate, L0_ffn_w_up, L0_ffn_w_down, L0_ffn_sw_gate, L0_ffn_sw_up, L0_ffn_sw_down, L0_ffn_w_shared_gate)
    return x

_drawn_inputs = setup_inputs


def setup_inputs(seed=0):
    import zlib

    import numpy as np

    out = dict(_drawn_inputs(seed))
    spreads = {}
    factors = {'L0_ffn_w_norm': 8.0,
     'L0_ffn_w_router': 8.0,
     'L0_ffn_w_gate': 8.0,
     'L0_ffn_w_up': 8.0,
     'L0_ffn_w_down': 8.0,
     'L0_ffn_sw_gate': 8.0,
     'L0_ffn_sw_up': 8.0,
     'L0_ffn_sw_down': 8.0,
     'L0_ffn_w_shared_gate': 8.0}
    for name, (base, spread) in spreads.items():
        noise = np.random.default_rng([zlib.crc32(name.encode()), seed]).standard_normal(out[name].shape)
        drawn = base * np.exp(spread * noise) if base else spread * noise
        out[name] = jnp.asarray(drawn.astype(out[name].dtype))
    for name, factor in factors.items():
        out[name] = (out[name] * factor).astype(out[name].dtype)
    return out
```

```python
import concourse.bass as bass
from concourse import mybir
from contextlib import ExitStack

F32, F32R, BF16, I32, U32 = mybir.dt.float32, mybir.dt.float32r, mybir.dt.bfloat16, mybir.dt.int32, mybir.dt.uint32
ALU, ACT, AX = mybir.AluOpType, mybir.ActivationFunctionType, mybir.AxisListType


def build(nc, x, ctx, g_xattn, g_ffn, ker, skip, w_norm, w_router, w_gate, w_up, w_down, sw_gate, sw_up,
          sw_down, w_sgate, out, filt_dram, slots_dram, yexp_dram):
    B, P, L = x.shape
    NHEAD = ker.shape[0]
    HD = P // NHEAD
    E, D, F = w_gate.shape
    FS = sw_gate.shape[1]
    TOPK, CAP = 4, 128
    EPS_LN, EPS_RMS = 1e-5, 1e-6
    GB = 2
    G = B // GB
    NB = L // P
    GC = NHEAD * GB * HD
    QH = 4
    UNITS = NB * NHEAD // QH
    HALF = F // 2
    NS = FS // F
    NR = E + 1
    RW, RX = 4, 2
    UN = 2 * RW
    FIRST = 6
    FILL, EXTRA = 2, 2
    U0 = FILL * NS + EXTRA
    ZROWS = E * CAP // P
    SKIP_ROW = 8192.0

    with ExitStack() as es:
        sb = lambda name, shape, dt=F32: es.enter_context(nc.sbuf_tensor(name, shape, dt))
        sem = lambda name: es.enter_context(nc.semaphore(name))
        bank = [es.enter_context(nc.psum_tensor(f"bank{i}", [P, 512], F32)) for i in range(8)]

        ident = sb("ident", [P, P])
        before = sb("before", [P, P], BF16)
        ones = sb("ones", [P, P], BF16)
        expert_no = sb("expert_no", [P, E])
        filt_pad = sb("filt_pad", [NHEAD, P + L])
        skip_sb = sb("skip_sb", [NHEAD, 1])
        gates = sb("gates", [P, 2])
        tanh_g = sb("tanh_g", [P, 2])
        gate_ident = sb("gate_ident", [P, P])
        primed = sb("primed", [NHEAD, 1])
        wnc = sb("wnc", [P, 2])
        wr = sb("wr", [P, 2, NR])
        wsg = sb("wsg", [P, 2])
        x_sb = sb("x_sb", [P, B, L])
        stats = sb("stats", [P, B, 6])
        mv = sb("mv", [P, B, 2])
        ve = sb("ve", [P, B])
        sd = sb("sd", [P, B])
        rq = sb("rq", [P, B])
        nbq = sb("nbq", [P, B])
        toep = sb("toep", [P, NHEAD, L])
        kv = sb("kv", [P, 2, NB, NHEAD, GB * HD * HD])
        prod = sb("prod", [P, 3, 512])
        oT = sb("oT", [P, 2, NB, GC])
        stats2 = sb("stats2", [P, GB, 6])
        mv2 = sb("mv2", [P, GB, 2])
        rv_in = sb("rv_in", [P, 2, GB])
        rv_sd = sb("rv_sd", [P, 2, GB])
        rv = sb("rv", [P, 2, GB])
        z_bias, b_scale, b_bias, b_gain = (sb(n, [P, GB]) for n in ("z_bias", "b_scale", "b_bias", "b_gain"))
        z = sb("z", [P, B, D])
        xnT = sb("xnT", [P, B, 2, P])
        zeros = sb("zeros", [P, D])
        top = sb("top", [P, B, 8])
        topi = sb("topi", [P, B, 8], U32)
        arg = sb("arg", [P, B, NR + TOPK])
        onehot = sb("onehot", [P, GB, TOPK, E])
        chosen = sb("chosen", [P, B, E], BF16)
        pick = sb("pick", [P, GB, TOPK, E])
        rowf, dropf = (sb(n, [P, GB, TOPK]) for n in ("rowf", "dropf"))
        pos, posc, kept, wtmp = (sb(n, [P, B, TOPK]) for n in ("pos", "posc", "kept", "wtmp"))
        sumr, rsum, half_tanh, sigm = (sb(n, [P, B]) for n in ("sumr", "rsum", "half_tanh", "sigm"))
        row_put = sb("row_put", [P, B * TOPK], I32)
        row_get = sb("row_get", [P, B * TOPK], I32)
        w_tok = sb("w_tok", [P, B, TOPK])
        w_sh = sb("w_sh", [P, B])
        sgu = [sb(n, [P, 2, 2, FS], F32R) for n in ("sgu_hi", "sgu_lo")]
        sdn = [sb(n, [HALF, NS, 2, D], F32R) for n in ("sdn_hi", "sdn_lo")]
        xs = [sb(n, [P, 2, 2, P], F32R) for n in ("xs_hi", "xs_lo")]
        aS = [sb(n, [HALF, 2, 2, P], F32R) for n in ("aS_hi", "aS_lo")]
        wgu = sb("wgu", [P, 2 * RW, 2, 2, F])
        wdn = sb("wdn", [HALF, 2 * RW, 2, D])
        act_g = sb("act_g", [P, 2, F])
        act_u = sb("act_u", [P, 2, F])
        ex = arg
        with ExitStack() as first_use:
            early = lambda name, shape: first_use.enter_context(nc.sbuf_tensor(name, shape, F32))
            ctx_sb = early("ctx_sb", [P, B, L])
            ctx_rev = early("ctx_rev", [P, 2, GB, NB, P])
            q_sb = early("q_sb", [P, 2, GB, L])
            cT = early("cT", [P, 2, NB, GC])
            qT = early("qT", [P, G, NB, GC])
        gu_parts = [sb(n, [P, 2, 2, 2, F], F32R) for n in ("wgu_hi", "wgu_lo")]
        xT_parts = [sb(n, [P, 2, 2, P], F32R) for n in ("xeT_hi", "xeT_lo")]
        sgu_raw = wgu[:].rearrange("p r n c f -> p (r n c f)")[:, 0:4 * FS].rearrange("p (n c f) -> p n c f", n=2, c=2)
        sdn_raw = wdn[:].rearrange("p r c d -> p (r c d)")[:, 0:NS * 2 * D].rearrange("p (s c d) -> p s c d", s=NS, c=2)
        toep_flat = toep[:].rearrange("p h l -> p (h l)")
        xe = toep_flat[:, 0:2 * RX * D].rearrange("p (n d) -> p n d", d=D)
        ye = toep_flat[:, 2 * RX * D:4 * RX * D].rearrange("p (n d) -> p n d", d=D)
        aT = toep_flat[0:HALF, 4 * RX * D + 4 * P:4 * RX * D + 8 * P].rearrange("p (u c t) -> p u c t", u=2, c=2)
        back = kv[:].rearrange("p g m h n -> p (g m h n)")[:, 0:B * TOPK * D].rearrange("p (t k d) -> p t k d", t=B, k=TOPK)

        def sems(names):
            return [sem(n) for n in names.split()]

        in_filt, in_gates, in_small, in_shared, filt_out, slots_zeroed, rows_put, out_done = sems(
            "in_filt in_gates in_small in_shared filt_out slots_zeroed rows_put out_done")
        in_ctx = [sem(f"in_ctx{g}") for g in range(G)]
        in_x = [sem(f"in_x{g}") for g in range(G)]
        in_toep = [sem(f"in_toep{i}") for i in range(NHEAD // QH)]
        in_w = [sem(f"in_w{i}") for i in range(RW)]
        in_xe = [sem(f"in_xe{i}") for i in range(RX)]
        y_out = [sem(f"y_out{i}") for i in range(RX)]
        in_back = [sem(f"in_back{i}") for i in range(2)]
        pool_step, consts, filt_ready, tanh_ready, gate_ready, wr_ready, split_hi, split_lo = sems(
            "pool_step consts filt_ready tanh_ready gate_ready wr_ready split_hi split_lo")
        dve_step, ve_ready, sd_ready, rq_ready, rev_ready, q_ready, t_in, t_out = sems(
            "dve_step ve_ready sd_ready rq_ready rev_ready q_ready t_in t_out")
        kv_ready, kv0_ready, unit_done, unit_read, oT_ready, oT_out = sems("kv_ready kv0_ready unit_done unit_read oT_ready oT_out")
        rv_ask, rv_got, norm_ready, gain_ready, z_ready, base_ready, xnT_out, xnT_ready, logits_done, arg_ready, ex_ready, half_ready = sems(
            "rv_ask rv_got norm_ready gain_ready z_ready base_ready xnT_out xnT_ready logits_done arg_ready ex_ready half_ready")
        chosen_ready, rank_done, route_ready = sems("chosen_ready rank_done route_ready")
        xt_done, x_hi, x_lo, w_hi, w_lo, gu_done, silu_done, a_ready, at_done, at_ready, dn_done, y_ready = sems(
            "xt_done x_hi x_lo w_hi w_lo gu_done silu_done a_ready at_done at_ready dn_done y_ready")
        xs_hi_ready, xs_ready, sgu_done, ssilu_done, sa_ready, sat_done, sat_hi, sat_ready, sdn_done, sy_read = sems(
            "xs_hi_ready xs_ready sgu_done ssilu_done sa_ready sat_done sat_hi sat_ready sdn_done sy_read")
        added, tile_ready = sems("added tile_ready")

        B_OUT = bank[2]
        B_XT = bank[7]
        B_LOG = B_RANK = bank[3]
        UB = [bank[6], bank[0], bank[1], bank[4], bank[5]]
        MORE = UNITS * G // 2
        unit_bank = lambda v: UB[1 + v % 4] if v < MORE else UB[(v - MORE) % 5]
        last_user = lambda v: v - 4 if v < MORE else v - 5
        prep_bank = lambda g, n: bank[2 + 4 * (g % 2) + n]

        def after(eng, semaphore, count, least):
            if not isinstance(count, int) or count >= least:
                eng.wait_ge(semaphore, count)

        block = es.enter_context(nc.Block())

        def w_load(eng, pair, slot):
            two = lambda w: w.rearrange("(n e) r f -> n e r f", e=2)[bass.ds(pair, 1)].rearrange(
                "n e (p c) f -> p (n e) (c f)", c=2)
            eng.dma_start(wgu[:, 2 * slot:2 * slot + 2, 0].rearrange("p e c f -> p e (c f)"), two(w_gate)).then_inc(in_w[slot], 16)
            eng.dma_start(wgu[:, 2 * slot:2 * slot + 2, 1].rearrange("p e c f -> p e (c f)"), two(w_up)).then_inc(in_w[slot], 16)
            eng.dma_start(wdn[:, 2 * slot:2 * slot + 2].rearrange("p e c f -> p e (c f)"), two(w_down)).then_inc(in_w[slot], 16)

        pair_rows = lambda t, pair: t.rearrange("(n e c) d -> n c e d", e=2, c=CAP)[bass.ds(pair, 1)].rearrange(
            "n c e d -> c (n e) d")

        @block.sync
        def _(sp):
            grp = lambda t, g: t[GB * g:GB * (g + 1)].rearrange("b p n -> p b n")
            sp.dma_start(filt_pad[:, P:], ker).then_inc(in_filt, 16)
            sp.dma_start(ctx_sb[:, 0:GB], grp(ctx, 0)).then_inc(in_ctx[0], 16)
            sp.dma_start(x_sb[:, 0:GB], grp(x, 0)).then_inc(in_x[0], 16)
            sp.wait_ge(filt_ready, 1)
            sp.dma_start(filt_dram, filt_pad[:]).then_inc(filt_out, 16)
            sp.dma_start(ctx_sb[:, GB:2 * GB], grp(ctx, 1)).then_inc(in_ctx[1], 16)
            sp.dma_start(x_sb[:, GB:2 * GB], grp(x, 1)).then_inc(in_x[1], 16)
            bc = lambda ap, n: bass.AP(tensor=ap.tensor, offset=ap.offset, ap=[[0, P], [1, n]])
            sp.dma_start(gates[:, 0:1], bc(g_xattn, 1)).then_inc(in_gates, 16)
            sp.dma_start(gates[:, 1:2], bc(g_ffn, 1)).then_inc(in_gates, 16)
            sp.wait_ge(filt_out, 16)
            for n in range(NHEAD // QH):
                sp.dma_start(toep[:, n * QH:(n + 1) * QH], bass.AP(
                    tensor=filt_dram.tensor, offset=1 + n * QH * (P + L), ap=[[1, P], [P + L, QH], [1, L]])).then_inc(in_toep[n], 16)
                if n < G - 2:
                    sp.dma_start(ctx_sb[:, GB * (n + 2):GB * (n + 3)], grp(ctx, n + 2)).then_inc(in_ctx[n + 2], 16)
                    sp.dma_start(x_sb[:, GB * (n + 2):GB * (n + 3)], grp(x, n + 2)).then_inc(in_x[n + 2], 16)
            sp.dma_start(wnc[:], w_norm.rearrange("(p c) -> p c", c=2)).then_inc(in_small, 16)
            sp.dma_start(wr[:, :, 0:E], w_router.rearrange("(p c) e -> p c e", c=2)).then_inc(in_small, 16)
            sp.dma_start(wsg[:], w_sgate.rearrange("(p c) e -> p (c e)", c=2)).then_inc(in_small, 16)
            sp.dma_start(sgu_raw[:, 0].rearrange("p c f -> p (c f)"), sw_gate.rearrange("(p c) f -> p (c f)", c=2)).then_inc(in_shared, 16)
            sp.dma_start(sgu_raw[:, 1].rearrange("p c f -> p (c f)"), sw_up.rearrange("(p c) f -> p (c f)", c=2)).then_inc(in_shared, 16)
            sp.dma_start(sdn_raw.rearrange("p s c d -> p s (c d)"), sw_down.rearrange("(s p c) d -> p s (c d)", s=NS, c=2)).then_inc(in_shared, 16)
            sp.wait_ge(pool_step, 3)
            sp.dma_start(slots_dram.rearrange("(p r) d -> p r d", r=ZROWS),
                         zeros[:].unsqueeze(1).broadcast_to((P, ZROWS, D))).then_inc(slots_zeroed, 16)
            sp.wait_ge(split_lo, 2)
            for pair in range(RW):
                w_load(sp, pair, pair)
            sp.wait_ge(rows_put, 16 * B * TOPK)

            def load_rows(pair, slot):
                sp.dma_start(xe[:, 2 * slot:2 * slot + 2], pair_rows(slots_dram, pair)).then_inc(in_xe[slot], 16)

            for pair in range(RX):
                load_rows(pair, pair)

            def pair_step(t, u, load_x=True, load_w=True, store=True):
                if load_x:
                    sp.wait_ge(xt_done, t * 2 + 2)
                    load_rows(t + 2, u % RX)
                if load_w:
                    sp.wait_ge(dn_done, t * 2)
                    w_load(sp, t + RW - 1, (u + RW - 1) % RW)
                if store:
                    n = (u + 1) % RX
                    sp.wait_ge(y_ready, t * 2)
                    sp.dma_start(pair_rows(yexp_dram, t - 1), ye[:, 2 * n:2 * n + 2]).then_inc(y_out[n], 16)

            NP = E // 2
            pair_step(0, 0, load_w=False, store=False)
            with sp.Fori(0, (NP - RW) // RW) as i:
                for u in range(RW):
                    pair_step(i * RW + (1 + u), (1 + u) % RW)
            for t in range(NP - RW + 1, NP + 1):
                pair_step(t, t % RW, load_x=t + 2 < NP, load_w=t + RW - 1 < NP)
            def store_tile(t):
                sp.dma_start(out[bass.ds(t, 1)].rearrange("o p n -> p (o n)"),
                             x_sb[:, bass.ds(t, 1)].rearrange("p o n -> p (o n)")).then_inc(out_done, 16)

            with sp.Fori(0, B - 1) as t:
                sp.wait_ge(tile_ready, t + 1)
                store_tile(t)
            sp.wait_ge(sy_read, B)
            store_tile(B - 1)
            sp.wait_ge(out_done, 16 * B)

        def products(eng, g, hh, done):
            for m in range(NB):
                half = cT[:, g % 2, m, hh * GC // 2:(hh + 1) * GC // 2].rearrange("p (n i) -> p n i", i=HD)
                n = GC // 2 // HD
                eng.tensor_tensor(
                    kv[:, g % 2, m, hh * NHEAD // 2:(hh + 1) * NHEAD // 2].rearrange("p h (b j i) -> p (h b) j i", b=GB, j=HD),
                    half.unsqueeze(3).broadcast_to((P, n, HD, HD)),
                    half.unsqueeze(2).broadcast_to((P, n, HD, HD)), ALU.mult).then_inc(done, 1)

        @block.gpsimd
        def _(pool):
            nc.gpsimd.memset(ident[:], 0.0).then_inc(pool_step, 1)
            nc.gpsimd.memset(before[:], 0.0).then_inc(pool_step, 1)
            nc.gpsimd.memset(zeros[:], 0.0).then_inc(pool_step, 1)
            nc.gpsimd.memset(ones[:], 1.0).then_inc(consts, 1)
            pool.wait_ge(pool_step, 3)
            nc.gpsimd.affine_select(out=ident[:], in_=ident[:], compare_op=ALU.not_equal, fill=1.0, base=0,
                                    pattern=[[-1, P]], channel_multiplier=1).then_inc(consts, 1)
            nc.gpsimd.affine_select(out=before[:], in_=before[:], compare_op=ALU.is_ge, fill=1.0, base=0,
                                    pattern=[[-1, P]], channel_multiplier=1).then_inc(consts, 1)
            nc.gpsimd.iota(expert_no[:], [[1, E]], base=0, channel_multiplier=0,
                           allow_small_or_imprecise_dtypes=True).then_inc(consts, 1)

            def group_products(g, halves):
                pool.wait_ge(t_out, 4 * g + 2)
                if g >= 2:
                    pool.wait_ge(unit_done, UNITS * (g - 1))
                for hh in halves:
                    products(nc.gpsimd, g, hh, kv_ready)

            def scatter(p):
                pool.wait_ge(route_ready, p + 1)
                for b in range(GB * p, GB * (p + 1)):
                    for k in range(TOPK):
                        c = b * TOPK + k
                        nc.gpsimd.indirect_dma_start(
                            slots_dram, bass.IndirectOffsetOnAxis(ap=row_put[:, c:c + 1], axis=0), z[:, b, :], None,
                            bounds_check=E * CAP - 1, oob_is_err=False).then_inc(rows_put, 16)

            group_products(0, (1,))
            group_products(1, (0, 1))
            group_products(2, (0, 1))
            pool.wait_ge(split_hi, 1)
            nc.gpsimd.tensor_tensor(sgu[1][:].rearrange("p n c f -> p (n c f)"), sgu_raw.rearrange("p n c f -> p (n c f)"),
                                    sgu[0][:].rearrange("p n c f -> p (n c f)").bitcast(F32), ALU.subtract).then_inc(split_lo, 1)
            group_products(3, (0, 1))
            pool.wait_ge(split_hi, 2)
            nc.gpsimd.tensor_tensor(sdn[1][:].rearrange("p s c d -> p (s c d)"), sdn_raw.rearrange("p s c d -> p (s c d)"),
                                    sdn[0][:].rearrange("p s c d -> p (s c d)").bitcast(F32), ALU.subtract).then_inc(split_lo, 1)
            pool.wait_ge(slots_zeroed, 16)
            for p in range(G):
                scatter(p)
            with pool.Fori(0, E // UN) as i:
                for u in range(UN):
                    pool.wait_ge(w_hi, i * UN + (u + 1))
                    nc.gpsimd.tensor_tensor(gu_parts[1][:, u % 2].rearrange("p n c f -> p (n c f)"),
                                            wgu[:, u].rearrange("p n c f -> p (n c f)"),
                                            gu_parts[0][:, u % 2].rearrange("p n c f -> p (n c f)").bitcast(F32), ALU.subtract).then_inc(w_lo, 1)
            for n in range(RX):
                pool.wait_ge(y_out[n], 16 * (E // 2 // RX))
            for t in range(B):
                if t >= 2:
                    pool.wait_ge(in_back[t % 2], 16 * TOPK * (t // 2))
                for k in range(TOPK):
                    c = t * TOPK + k
                    nc.gpsimd.indirect_dma_start(back[:, t, k], None, yexp_dram, bass.IndirectOffsetOnAxis(
                        ap=row_get[:, c:c + 1], axis=0)).then_inc(in_back[t % 2], 16)

        @block.scalar
        def _(act):
            A = nc.scalar.activation
            act.dma_start(skip_sb[:], skip.rearrange("(h o) -> h o", o=1)).then_inc(in_filt, 16)

            def reverse(g):
                act.wait_ge(in_ctx[g], 16)
                if g >= 2:
                    act.wait_ge(t_in, 2 * (g - 2) + 1)
                A(ctx_rev[:, g % 2].rearrange("p b m t -> p (b m) t"),
                  ctx_sb[:, GB * g:GB * (g + 1)].rearrange("p b (m t) -> p (b m) t", m=NB)[:, :, ::-1], ACT.Copy).then_inc(rev_ready, 1)

            def root(n, gs):
                act.wait_ge(ve_ready, n)
                A(sd[:, gs], ve[:, gs], ACT.Sqrt).then_inc(sd_ready, 1)

            def normalise(g):
                act.wait_ge(rq_ready, 2 if g else 1)
                if g >= 2:
                    act.wait_ge(t_in, 2 * (g - 1))
                for j in range(GB):
                    b = GB * g + j
                    A(q_sb[:, g % 2, j], x_sb[:, b], ACT.Identity, bias=nbq[:, b:b + 1], scale=rq[:, b:b + 1]).then_inc(q_ready, 1)

            def transposed_out(g, n):
                act.wait_ge(t_in, 2 * g + n + 1)
                if g >= 2 and n == 0:
                    act.wait_ge(kv_ready, 4 * (g - 1) - 2)
                    act.wait_ge(kv0_ready, NB)
                dst = qT[:, g] if n else cT[:, g % 2]
                hb = QH * HD if n else HD
                for m in range(NB):
                    A(dst[:, m].rearrange("p (h b i) -> p b h i", b=GB, i=hb),
                      prep_bank(g, n)[:, m * GB * P:(m + 1) * GB * P].rearrange("p (b h i) -> p b h i", b=GB, i=hb),
                      ACT.Copy).then_inc(t_out, 1)

            act.wait_ge(dve_step, 1)
            A(primed[:], filt_pad[:, 0:1], ACT.Sqrt)
            reverse(0)
            transposed_out(0, 0)
            root(1, slice(0, GB))
            normalise(0)
            reverse(1)
            transposed_out(0, 1)
            transposed_out(1, 0)
            act.wait_ge(in_gates, 32)
            A(tanh_g[:], gates[:], ACT.Tanh).then_inc(tanh_ready, 1)
            reverse(2)
            root(2, slice(GB, B))
            normalise(1)
            normalise(2)
            transposed_out(1, 1)
            transposed_out(2, 0)
            reverse(3)
            normalise(3)
            transposed_out(2, 1)
            transposed_out(3, 0)
            transposed_out(3, 1)
            act.wait_ge(in_shared, 48)
            A(sgu[0][:].rearrange("p n c f -> p (n c f)"), sgu_raw.rearrange("p n c f -> p (n c f)"), ACT.Copy).then_inc(split_hi, 1)
            A(sdn[0][:].rearrange("p s c d -> p (s c d)"), sdn_raw.rearrange("p s c d -> p (s c d)"), ACT.Copy).then_inc(split_hi, 1)
            act.wait_ge(in_small, 16 * 3)
            A(wr[:, :, E], wsg[:], ACT.Copy).then_inc(wr_ready, 1)

            def roots(p):
                act.wait_ge(rv_ask, 2 * (p + 1))
                A(rv_sd[:], rv_in[:], ACT.Sqrt).then_inc(rv_got, 1)

            def rows(p):
                act.wait_ge(norm_ready, p + 1)
                for j in range(GB):
                    A(z[:, GB * p + j], B_OUT[:, j * L:(j + 1) * L], ACT.Identity, bias=z_bias[:, j:j + 1],
                      scale=rv[:, 1, j:j + 1]).then_inc(z_ready, 1)

            def base(p):
                act.wait_ge(gain_ready, 2 * (p + 1))
                for j in range(GB):
                    A(x_sb[:, GB * p + j], B_OUT[:, j * L:(j + 1) * L], ACT.Identity, bias=b_bias[:, j:j + 1],
                      scale=b_scale[:, j:j + 1]).then_inc(base_ready, 1)

            def rows_T_out(p):
                act.wait_ge(xnT_out, p + 1)
                for c in range(2):
                    A(xnT[:, GB * p:GB * (p + 1), c], B_XT[:].rearrange("p (b c t) -> p b c t", b=GB, c=2)[:, :, c], ACT.Copy,
                      scale=wnc[:, c:c + 1]).then_inc(xnT_ready, 1)

            def exps():
                act.wait_ge(arg_ready, 2)
                A(ex[:, :, 0:E], arg[:, :, 0:E], ACT.Exp).then_inc(ex_ready, 1)
                A(ex[:, :, NR:], arg[:, :, NR:], ACT.Exp).then_inc(ex_ready, 1)

            def stage(t, u):
                after(act, sgu_done, NS * (t - 1), NS)
                A(xs[0][:, u].rearrange("p c t -> p (c t)"), xnT[:, bass.ds(t, 1)].rearrange("p o c t -> p (o c t)"),
                  ACT.Copy).then_inc(xs_hi_ready, 1)

            def sh_silu(v, u):
                act.wait_ge(sgu_done, v + 1)
                after(act, sa_ready, v - 1, 1)
                A(act_g[:, u], bank[u][:, 0:F], ACT.Silu).then_inc(ssilu_done, 1)

            def sh_aT(v, u):
                act.wait_ge(sat_done, v + 1)
                after(act, sdn_done, v - 1, 1)
                A(aS[0][:, u].rearrange("p c t -> p (c t)"), bank[4 + u][0:HALF, 0:2 * P], ACT.Copy).then_inc(sat_hi, 1)

            def ex_w(e, pair, n):
                slot = n // 2
                if n % 2 == 0:
                    act.wait_ge(in_w[slot], (pair - slot) * (48 // RW) + 48)
                after(act, gu_done, e - 1, 1)
                A(gu_parts[0][:, n % 2].rearrange("p n c f -> p (n c f)"), wgu[:, n].rearrange("p n c f -> p (n c f)"),
                  ACT.Copy).then_inc(w_hi, 1)

            for p in range(G - 1):
                if p == G - 2:
                    stage(0, 0)
                    stage(1, 1)
                roots(p)
                rows(p)
                if p < G - 2:
                    base(p)
                rows_T_out(p)
                if p == G - 2:
                    base(p)
            sh_silu(0, 0)
            sh_silu(1, 1)
            roots(G - 1)
            sh_aT(0, 0)
            sh_aT(1, 1)
            rows(G - 1)
            rows_T_out(G - 1)
            sh_silu(2, 0)
            sh_silu(3, 1)
            base(G - 1)
            sh_aT(2, 0)
            for v in range(NS, U0):
                if v == NS:
                    act.wait_ge(chosen_ready, G)
                    A(half_tanh[:], arg[:, :, E], ACT.Tanh, scale=0.5).then_inc(half_ready, 1)
                if v == FILL * NS:
                    stage(FILL + 1, (FILL + 1) % 2)
                sh_silu(v, v % 2)
                sh_aT(v - 1, 1 - v % 2)
                if v == NS + 1:
                    stage(FILL, FILL % 2)
                if v in (NS, NS + 2):
                    ex_w((v - NS) // 2, 0, (v - NS) // 2)
            exps()
            sh_aT(U0 - 1, 1)

            def ex_xT(e, u):
                act.wait_ge(xt_done, e + 1)
                after(act, gu_done, e - 1, 1)
                for c in range(2):
                    A(xT_parts[0][:, u, c], bank[2 + u][:, c * P:(c + 1) * P], ACT.Copy, scale=wnc[:, c:c + 1]).then_inc(x_hi, 1)

            def ex_silu(e, u):
                act.wait_ge(gu_done, e + 1)
                if isinstance(e, int) and e < 2:
                    act.wait_ge(sa_ready, U0)
                else:
                    act.wait_ge(a_ready, e - 1)
                A(act_g[:, u], bank[u][:, 0:F], ACT.Silu).then_inc(silu_done, 1)

            def ex_y(e, pair, n):
                act.wait_ge(dn_done, e + 1)
                slot = n // 2
                after(act, y_out[slot], (pair - slot) * (16 // RX), 1)
                A(ye[:, n], bank[7][:, 0:D], ACT.Copy).then_inc(y_ready, 1)

            def ex_step(t, pair, c, xt=True, gu=True, w=True, y=True):
                if xt:
                    ex_xT(t + 1, (c + 1) % 2)
                if gu:
                    ex_silu(t, c % 2)
                if w:
                    ex_w(t + 2, pair + 1, (c + 2) % UN)
                if y:
                    ex_y(t - 2, pair - 1, (c - 2) % (2 * RX))

            ex_xT(0, 0)
            for t in range(FIRST):
                ex_step(t, t // 2, t, y=t >= 2)
            with act.Fori(0, (E - UN) // UN) as i:
                for u in range(UN):
                    ex_step(i * UN + (FIRST + u), i * (UN // 2) + (FIRST + u) // 2, (FIRST + u) % UN)
            for t in range(E - UN + FIRST, E + 2):
                ex_step(t, t // 2, t % UN, xt=t + 1 < E, gu=t < E, w=False)
                if t == E:
                    act.wait_ge(a_ready, E)
                    sh_silu(U0, 0)
            for s in range(EXTRA + 1, NS):
                v = FILL * NS + s
                sh_silu(v, s % 2)
                sh_aT(v - 1, (s - 1) % 2)

            def sh_tile(t, par, more):
                for s in range(NS):
                    sh_silu(t * NS + s, s % 2)
                    sh_aT(t * NS + (s - 1), (s + 1) % 2)
                    if s == 0 and more:
                        stage(t + 1, 1 - par)

            with act.Fori(0, (B - FILL - 2) // 2) as i:
                for u in range(2):
                    sh_tile(i * 2 + (FILL + 1 + u), (FILL + 1 + u) % 2, True)
            sh_tile(B - 1, (B - 1) % 2, False)
            sh_aT(B * NS - 1, 1)

        @block.vector
        def _(dve):
            V = nc.vector
            steps = [0]

            def step(ins):
                steps[0] += 1
                ins.then_inc(dve_step, 1)

            def settle():
                dve.wait_ge(dve_step, steps[0])

            step(V.memset(filt_pad[:, 0:P], 0.0))
            settle()
            dve.wait_ge(in_filt, 32)
            V.tensor_tensor(filt_pad[:, P:P + 1], filt_pad[:, P:P + 1], skip_sb[:], ALU.add).then_inc(filt_ready, 1)

            def q_stats(g):
                dve.wait_ge(in_x[g], 16)
                for b in range(GB * g, GB * (g + 1)):
                    step(V.bn_stats(stats[:, b], x_sb[:, b]))

            def q_ask(first, last):
                gs = slice(GB * first, GB * (last + 1))
                settle()
                for b in range(gs.start, gs.stop):
                    step(V.bn_aggr(mv[:, b], stats[:, b]))
                settle()
                V.tensor_scalar(ve[:, gs], mv[:, gs, 1], EPS_LN, None, ALU.add).then_inc(ve_ready, 1)

            def q_scales(n, first, last):
                gs = slice(GB * first, GB * (last + 1))
                dve.wait_ge(sd_ready, n)
                step(V.reciprocal(rq[:, gs], sd[:, gs]))
                settle()
                V.scalar_tensor_tensor(out=nbq[:, gs], in0=mv[:, gs, 0], scalar=-1.0, in1=rq[:, gs], op0=ALU.mult,
                                       op1=ALU.mult).then_inc(rq_ready, 1)

            def unit_mul(g, n):
                hq, lb = n // NB, n % NB
                v = UNITS * g + n
                dve.wait_ge(unit_done, v + 1)
                if n == 0:
                    dve.wait_ge(t_out, 4 * (g + 1))
                if v >= 3:
                    dve.wait_ge(oT_ready, v - 2)
                ncols = QH * GB
                q = qT[:, g, lb, hq * ncols * HD:(hq + 1) * ncols * HD].rearrange("p (n i) -> p n i", i=HD)
                V.tensor_tensor(prod[:, v % 3].rearrange("p (n j i) -> p n j i", j=HD, i=HD),
                                unit_bank(v)[:].rearrange("p (n j i) -> p n j i", j=HD, i=HD),
                                q.unsqueeze(2).broadcast_to((P, ncols, HD, HD)), ALU.mult).then_inc(unit_read, 1)

            def unit_sum(g, n):
                hq, lb = n // NB, n % NB
                v = UNITS * g + n
                dve.wait_ge(unit_read, v + 1)
                V.tensor_reduce(oT[:, g % 2, lb].rearrange("p (b n) -> p b n", b=GB)[:, :, hq * QH * HD:(hq + 1) * QH * HD],
                                prod[:, v % 3].rearrange("p (b n i) -> p b n i", b=GB, i=HD), AX.X, ALU.add).then_inc(oT_ready, 1)

            def out_stats(p):
                dve.wait_ge(oT_out, p + 1)
                for j in range(GB):
                    step(V.bn_stats(stats2[:, j], B_OUT[:, j * L:(j + 1) * L]))
                settle()
                for j in range(GB):
                    step(V.bn_aggr(mv2[:, j], stats2[:, j]))
                settle()
                V.tensor_scalar(rv_in[:, 0], mv2[:, :, 1], EPS_LN, None, ALU.add).then_inc(rv_ask, 1)
                V.tensor_scalar(rv_in[:, 1], mv2[:, :, 1], 1.0 + EPS_RMS, EPS_LN * EPS_RMS, ALU.mult, ALU.add).then_inc(rv_ask, 1)

            def norms(p):
                dve.wait_ge(rv_got, p + 1)
                if p:
                    dve.wait_ge(base_ready, GB * p)
                step(V.reciprocal(rv[:], rv_sd[:]))
                settle()
                V.scalar_tensor_tensor(out=z_bias[:], in0=mv2[:, :, 0], scalar=-1.0, in1=rv[:, 1], op0=ALU.mult,
                                       op1=ALU.mult).then_inc(norm_ready, 1)
                if p == 0:
                    dve.wait_ge(tanh_ready, 1)
                step(V.tensor_scalar(b_gain[:], rv[:, 0], tanh_g[:, 1:2], None, ALU.mult))
                settle()
                V.tensor_scalar(b_scale[:], b_gain[:], 1.0, None, ALU.add).then_inc(gain_ready, 1)
                V.scalar_tensor_tensor(out=b_bias[:], in0=mv2[:, :, 0], scalar=-1.0, in1=b_gain[:], op0=ALU.mult,
                                       op1=ALU.mult).then_inc(gain_ready, 1)

            def choose(p):
                dve.wait_ge(logits_done, p + 1)
                ps = slice(GB * p, GB * (p + 1))
                log = B_LOG[:, 0:GB * 64].rearrange("p (b n) -> p b n", b=GB)
                for j in range(GB):
                    step(V.max(top[:, GB * p + j], log[:, j, 0:E]))
                step(V.tensor_copy(arg[:, ps, 0:NR], log[:, :, 0:NR]))
                settle()
                for j in range(GB):
                    step(V.max_index(topi[:, GB * p + j], top[:, GB * p + j], log[:, j, 0:E]))
                settle()
                step(V.tensor_tensor(onehot[:], expert_no[:].unsqueeze(1).unsqueeze(1).broadcast_to((P, GB, TOPK, E)),
                                     topi[:, ps, 0:TOPK].unsqueeze(3).broadcast_to((P, GB, TOPK, E)), ALU.is_equal))
                settle()
                with nc.allow_low_precision(reason="counts of at most one"):
                    V.tensor_reduce(chosen[:, ps], onehot[:].rearrange("p b k e -> p b e k"), AX.X, ALU.add).then_inc(chosen_ready, 1)

            def place(p):
                dve.wait_ge(rank_done, p + 1)
                ps = slice(GB * p, GB * (p + 1))
                rank = B_RANK[:, 0:GB * 64].rearrange("p (b n) -> p b n", b=GB)
                step(V.tensor_tensor(pick[:], onehot[:], rank[:, :, 0:E].unsqueeze(2).broadcast_to((P, GB, TOPK, E)), ALU.mult))
                settle()
                step(V.tensor_reduce(pos[:, ps], pick[:], AX.X, ALU.add))
                settle()
                step(V.scalar_tensor_tensor(out=rowf[:], in0=topi[:, ps, 0:TOPK], scalar=float(CAP), in1=pos[:, ps],
                                            op0=ALU.mult, op1=ALU.add))
                step(V.tensor_scalar(dropf[:], pos[:, ps], float(CAP), SKIP_ROW, ALU.is_ge, ALU.mult))
                settle()
                V.tensor_tensor(row_put[:, GB * TOPK * p:GB * TOPK * (p + 1)].rearrange("p (b k) -> p b k", b=GB), rowf[:],
                                dropf[:], ALU.add).then_inc(route_ready, 1)

            def arguments():
                V.tensor_tensor(arg[:, :, 0:E], arg[:, :, 0:E], top[:, :, 0:1].broadcast_to((P, B, E)), ALU.subtract).then_inc(arg_ready, 1)
                V.tensor_tensor(arg[:, :, NR:], top[:, :, 0:TOPK], top[:, :, 0:1].broadcast_to((P, B, TOPK)),
                                ALU.subtract).then_inc(arg_ready, 1)

            def gather_rows():
                step(V.tensor_scalar(posc[:], pos[:], float(CAP - 1), None, ALU.min))
                step(V.tensor_scalar(kept[:], pos[:], float(CAP), None, ALU.is_lt))
                settle()
                step(V.scalar_tensor_tensor(out=row_get[:].rearrange("p (b k) -> p b k", b=B), in0=topi[:, :, 0:TOPK],
                                            scalar=float(CAP), in1=posc[:], op0=ALU.mult, op1=ALU.add))

            def shared_gate():
                dve.wait_ge(half_ready, 1)
                step(V.tensor_scalar(sigm[:], half_tanh[:], 0.5, 0.5, ALU.mult, ALU.add))
                settle()
                step(V.tensor_scalar(w_sh[:], sigm[:], tanh_g[:, 1:2], None, ALU.mult))
                settle()
                dve.wait_ge(base_ready, GB * G)

            def weights():
                dve.wait_ge(ex_ready, 2)
                step(V.tensor_reduce(sumr[:], ex[:, :, 0:E], AX.X, ALU.add))
                settle()
                step(V.scalar_tensor_tensor(out=wtmp[:], in0=ex[:, :, NR:], scalar=tanh_g[:, 1:2], in1=kept[:], op0=ALU.mult, op1=ALU.mult))
                step(V.reciprocal(rsum[:], sumr[:]))
                settle()
                step(V.tensor_tensor(w_tok[:], wtmp[:], rsum[:].unsqueeze(2).broadcast_to((P, B, TOPK)), ALU.mult))
                settle()

            def stage_lo(t, u):
                dve.wait_ge(xs_hi_ready, t + 1)
                V.tensor_tensor(xs[1][:, u].rearrange("p c t -> p (c t)"), xnT[:, bass.ds(t, 1)].rearrange("p o c t -> p (o c t)"),
                                xs[0][:, u].rearrange("p c t -> p (c t)").bitcast(F32), ALU.subtract).then_inc(xs_ready, 1)

            def sh_mul(v, u):
                dve.wait_ge(ssilu_done, v + 1)
                after(dve, sat_done, v - 1, 1)
                V.tensor_tensor(act_u[:, u], act_g[:, u], bank[u][:, F:2 * F], ALU.mult).then_inc(sa_ready, 1)

            def sh_aT(v, u):
                dve.wait_ge(sat_hi, v + 1)
                V.tensor_tensor(aS[1][:, u].rearrange("p c t -> p (c t)"), bank[4 + u][0:HALF, 0:2 * P],
                                aS[0][:, u].rearrange("p c t -> p (c t)").bitcast(F32), ALU.subtract).then_inc(sat_ready, 1)

            def sh_y(t, u):
                dve.wait_ge(sdn_done, t * NS + NS)
                row = x_sb[:, bass.ds(t, 1)].rearrange("p o n -> p (o n)")
                V.scalar_tensor_tensor(out=row, in0=bank[6 + u][:, 0:D], scalar=w_sh[:, bass.ds(t, 1)], in1=row,
                                       op0=ALU.mult, op1=ALU.add).then_inc(sy_read, 1)

            def ex_xT(e, u):
                dve.wait_ge(x_hi, e * 2 + 2)
                for c in range(2):
                    V.scalar_tensor_tensor(out=xT_parts[1][:, u, c], in0=bank[2 + u][:, c * P:(c + 1) * P], scalar=wnc[:, c:c + 1],
                                           in1=xT_parts[0][:, u, c].bitcast(F32), op0=ALU.mult, op1=ALU.subtract).then_inc(x_lo, 1)

            q_stats(0)
            q_ask(0, 0)
            q_scales(1, 0, 0)
            dve.wait_ge(t_out, 2)
            products(V, 0, 0, kv0_ready)
            q_stats(1)
            q_stats(2)
            for g in range(G):
                for n in range(UNITS):
                    unit_mul(g, n)
                    if g or n:
                        unit_sum(g, n - 1) if n else unit_sum(g - 1, UNITS - 1)
                    if g == 0 and n == 0:
                        q_stats(3)
                        q_ask(1, G - 1)
                    if g == 0 and n == 1:
                        q_scales(2, 1, G - 1)
                    if g == 0 and n == 6:
                        dve.wait_ge(tanh_ready, 1)
                        V.tensor_scalar(gate_ident[:], ident[:], tanh_g[:, 0:1], None, ALU.mult).then_inc(gate_ready, 1)
                    if g == 2 and n == 1:
                        choose(0)
                    if g == G - 1 and n == 1:
                        place(g - 2)
                    if g and n == (2 if g > 1 else 3):
                        out_stats(g - 1)
                    if g and n == (3 if g > 1 else 4):
                        norms(g - 1)
                    if g == 2 and n == 4:
                        place(0)
                    if g >= 2 and n == (7 if g < G - 1 else 6):
                        choose(g - 1)
                    if g == G - 1 and n in (3, 4):
                        stage_lo(n - 3, n - 3)
            unit_sum(G - 1, UNITS - 1)
            sh_mul(0, 0)
            place(G - 2)
            out_stats(G - 1)
            sh_mul(1, 1)
            norms(G - 1)
            sh_aT(0, 0)
            sh_aT(1, 1)
            choose(G - 1)
            sh_mul(2, 0)
            place(G - 1)
            sh_mul(3, 1)
            sh_aT(2, 0)
            for v in range(NS, U0):
                if v == FILL * NS:
                    stage_lo(FILL + 1, (FILL + 1) % 2)
                sh_mul(v, v % 2)
                sh_aT(v - 1, 1 - v % 2)
                if v == NS:
                    arguments()
                if v == NS + 2:
                    gather_rows()
                    shared_gate()
                if v == NS + 3:
                    sh_y(0, 0)
                if v == NS + 1:
                    stage_lo(FILL, FILL % 2)
            sh_aT(U0 - 1, 1)
            ex_xT(0, 0)
            ex_xT(1, 1)

            def ex_mul(e, u):
                dve.wait_ge(silu_done, e + 1)
                after(dve, at_done, e - 1, 1)
                V.tensor_tensor(act_u[:, u], act_g[:, u], bank[u][:, F:2 * F], ALU.mult).then_inc(a_ready, 1)

            def ex_aT(e, u):
                dve.wait_ge(at_done, e + 1)
                after(dve, dn_done, e - 1, 1)
                V.tensor_copy(aT[:, u].rearrange("p c t -> p (c t)"), bank[4 + u][0:HALF, 0:2 * P]).then_inc(at_ready, 1)

            ex_mul(0, 0)
            weights()
            for t in range(1, 4):
                ex_xT(t + 1, (t + 1) % 2)
                ex_mul(t, t % 2)
                ex_aT(t - 1, (t - 1) % 2)
                if t == 1:
                    for s in range(1, FILL):
                        sh_y(s, s % 2)
            with dve.Fori(0, (E - 6) // 2) as i:
                for u in range(2):
                    ex_xT(i * 2 + (5 + u), 1 - u)
                    ex_mul(i * 2 + (4 + u), u)
                    ex_aT(i * 2 + (3 + u), 1 - u)
            ex_xT(E - 1, 1)
            for t in range(E - 2, E):
                ex_mul(t, t % 2)
                ex_aT(t - 1, (t - 1) % 2)
            ex_aT(E - 1, 1)

            def add_row(t, u, k, count):
                if k == 0:
                    dve.wait_ge(in_back[u], (t - u) * (16 * TOPK // 2) + 16 * TOPK)
                    if not isinstance(t, int) or t < B - 1:
                        dve.wait_ge(sy_read, t + 1)
                else:
                    dve.wait_ge(added, count)
                row = x_sb[:, bass.ds(t, 1)].rearrange("p o n -> p (o n)")
                last = k == TOPK - 1 and not (isinstance(t, int) and t == B - 1)
                V.scalar_tensor_tensor(out=row, in0=back[:, bass.ds(t, 1), k].rearrange("p o n -> p (o n)"),
                                       scalar=w_tok[:, bass.ds(t, 1), k:k + 1].rearrange("p o k -> p (o k)"),
                                       in1=row, op0=ALU.mult, op1=ALU.add).then_inc(tile_ready if last else added, 1)

            def sh_tile(t, par, adds):
                for s in range(NS):
                    sh_mul(t * NS + s, s % 2)
                    add_next(adds[s] // 2)
                    sh_aT(t * NS + (s - 1), (s + 1) % 2)
                    if s == 0 and t < B - 1:
                        stage_lo(t + 1, 1 - par)
                    if s == 1:
                        sh_y(t - 1, 1 - par)
                    add_next(adds[s] - adds[s] // 2)

            left = [(t, k) for t in range(B) for k in range(TOPK)]
            count_added = [0]

            def add_next(n):
                for _ in range(n):
                    t, k = left.pop(0)
                    add_row(t, t % 2, k, count_added[0])
                    if k < TOPK - 1 or t == B - 1:
                        count_added[0] += 1

            sh_mul(U0, 0)
            for s in range(EXTRA + 1, NS):
                v = FILL * NS + s
                sh_mul(v, s % 2)
                sh_aT(v - 1, (s - 1) % 2)
            ADDS = ((0, 0, 0, 0), (2, 2, 2, 2), (1, 1, 2, 2), (2, 2, 2, 2), (2, 0, 2, 2))
            for t, adds in zip(range(FILL + 1, B), ADDS):
                sh_tile(t, t % 2, adds)
            add_next(2)
            sh_aT(B * NS - 1, 1)
            add_next(len(left))
            dve.wait_ge(added, count_added[0])
            sh_y(B - 1, (B - 1) % 2)

        @block.tensor
        def _(pe):
            T = nc.tensor
            pe.wait_ge(consts, 4)

            def prepare_T(g, n):
                pe.wait_ge(q_ready, GB * (g + 1)) if n else pe.wait_ge(rev_ready, g + 1)
                if g >= 2:
                    pe.wait_ge(t_out, 4 * (g - 2) + 2 * (n + 1))
                for m in range(NB):
                    for j in range(GB):
                        src = q_sb[:, g % 2, j, m * P:(m + 1) * P] if n else ctx_rev[:, g % 2, j, m]
                        last = T.transpose(prep_bank(g, n)[:, (m * GB + j) * P:(m * GB + j + 1) * P], src, ident[:])
                last.then_inc(t_in, 1)

            def unit(g, n):
                hq, lb = n // NB, n % NB
                v = UNITS * g + n
                second = hq * QH * 2 // NHEAD
                if g == 0:
                    pe.wait_ge(kv_ready, NB) if second else pe.wait_ge(kv0_ready, NB)
                    pe.wait_ge(in_toep[hq], 16)
                else:
                    pe.wait_ge(kv_ready, NB * (2 * g + second))
                if last_user(v) >= 0 and v != MORE:
                    pe.wait_ge(unit_read, last_user(v) + 1)
                for h in range(QH):
                    head = hq * QH + h
                    for m in range(lb + 1):
                        o = unit_bank(v)[:].rearrange("p (b h n) -> p b h n", b=GB, h=QH)[:, :, h]
                        last = T.matmul(o, toep[:, head, (lb - m) * P:(lb - m + 1) * P],
                                        kv[:, g % 2, m, head].rearrange("p (b n) -> p b n", b=GB), start=(m == 0), stop=(m == lb))
                last.then_inc(unit_done, 1)

            def out_x(p):
                if p == 0:
                    pe.wait_ge(t_out, 4 * G)
                else:
                    pe.wait_ge(base_ready, GB * p)
                T.matmul(B_OUT[:], ident[:], x_sb[:, GB * p:GB * (p + 1)].rearrange("p b l -> p (b l)"), start=True, stop=False)

            def out_T(p):
                if p == 0:
                    pe.wait_ge(gate_ready, 1)
                pe.wait_ge(oT_ready, UNITS * (p + 1))
                for j in range(GB):
                    for lb in range(NB):
                        last = T.matmul(B_OUT[:, (j * NB + lb) * P:(j * NB + lb + 1) * P],
                                        oT[:, p % 2, lb, j * P:(j + 1) * P], gate_ident[:], start=False,
                                        stop=(j == GB - 1 and lb == NB - 1))
                last.then_inc(oT_out, 1)

            def rows_T(p):
                pe.wait_ge(z_ready, GB * (p + 1))
                for j in range(GB):
                    for c in range(2):
                        last = T.transpose(B_XT[:, (j * 2 + c) * P:(j * 2 + c + 1) * P],
                                           z[:, GB * p + j].rearrange("p (d c) -> p c d", c=2)[:, c], ident[:])
                last.then_inc(xnT_out, 1)

            def logits(p):
                pe.wait_ge(xnT_ready, 2 * (p + 1))
                pe.wait_ge(wr_ready, 1)
                if p:
                    pe.wait_ge(route_ready, p)
                for j in range(GB):
                    for c in range(2):
                        last = T.matmul(B_LOG[:, j * 64:j * 64 + NR], xnT[:, GB * p + j, c], wr[:, c], start=(c == 0), stop=(c == 1))
                last.then_inc(logits_done, 1)

            def ranks(p):
                pe.wait_ge(chosen_ready, p + 1)
                for j in range(GB):
                    b = GB * p + j
                    o = B_RANK[:, j * 64:j * 64 + E]
                    for s in range(b):
                        T.matmul(o, ones[:], chosen[:, s], start=(s == 0), stop=False)
                    last = T.matmul(o, before[:], chosen[:, b], start=(b == 0), stop=True)
                last.then_inc(rank_done, 1)

            PARTS = ((0, 0), (0, 1), (1, 0))

            def sh_gu(v, u, par, s):
                after(pe, sa_ready, v - 1, 1)
                for c in range(2):
                    for n, (a, w) in enumerate(PARTS):
                        last = T.matmul(bank[u][:, 0:2 * F].rearrange("p (n f) -> p n f", n=2), xs[a][:, par, c],
                                        sgu[w][:, :, c, s * F:(s + 1) * F], start=(c == 0 and n == 0), stop=(c == 1 and n == 2))
                last.then_inc(sgu_done, 1)

            def sh_at(v, u):
                pe.wait_ge(sa_ready, v + 1)
                after(pe, sat_ready, v - 1, 1)
                for c in range(2):
                    last = T.transpose(bank[4 + u][0:HALF, c * P:(c + 1) * P],
                                       act_u[:, u].rearrange("p (f c) -> p c f", c=2)[:, c], ident[:])
                last.then_inc(sat_done, 1)

            def sh_dn(t, v, u, par, s):
                pe.wait_ge(sat_ready, v + 1)
                if s == 0:
                    after(pe, sy_read, t - 1, 1)
                for c in range(2):
                    for n, (a, w) in enumerate(PARTS):
                        last = T.matmul(bank[6 + par][:, 0:D], aS[a][:, u, c], sdn[w][:, s, c], start=(s == 0 and c == 0 and n == 0),
                                        stop=(s == NS - 1 and c == 1 and n == 2))
                last.then_inc(sdn_done, 1)

            def sh_unit(t, par, s, under_way=2):
                v = t * NS + s
                if s == 0:
                    pe.wait_ge(xs_ready, t + 1)
                sh_gu(v, s % 2, par, s)
                if under_way > 0:
                    sh_at(v - 1, (s - 1) % 2)
                if under_way > 1 and s >= 2:
                    sh_dn(t, v - 2, s % 2, par, s - 2)
                elif under_way > 1:
                    sh_dn(t - 1, v - 2, s % 2, 1 - par, s + 2)

            def sh_end(v, t, par, s):
                sh_dn(t, v - 1, (s - 1) % 2, par, s - 1)
                sh_at(v, s % 2)
                sh_dn(t, v, s % 2, par, s)

            prepare_T(0, 0)
            prepare_T(0, 1)
            prepare_T(1, 0)
            for g in range(G):
                for n in range(UNITS):
                    unit(g, n)
                    if g == 0 and n == 4:
                        prepare_T(1, 1)
                        prepare_T(2, 0)
                    if g == 0 and n == 6:
                        prepare_T(2, 1)
                        prepare_T(3, 0)
                    if g == 1 and n == 0:
                        prepare_T(3, 1)
                    if g >= 2 and n == 1:
                        rows_T(g - 2)
                    if g >= 2 and n == 2:
                        logits(g - 2)
                    if g >= 2 and n == (3 if g > 2 else 5):
                        ranks(g - 2)
                    if g and n == 3:
                        out_x(g - 1)
                        out_T(g - 1)
            LAST = UNITS * G
            rows_T(G - 2)
            pe.wait_ge(split_lo, 2)
            pe.wait_ge(xs_ready, 1)
            pe.wait_ge(unit_read, LAST - 4)
            sh_gu(0, 0, 0, 0)
            logits(G - 2)
            pe.wait_ge(unit_read, LAST - 3)
            sh_gu(1, 1, 0, 1)
            out_x(G - 1)
            ranks(G - 2)
            out_T(G - 1)
            sh_at(0, 0)
            sh_gu(2, 0, 0, 2)
            sh_at(1, 1)
            sh_gu(3, 1, 0, 3)
            rows_T(G - 1)
            sh_dn(0, 0, 0, 0, 0)
            logits(G - 1)
            sh_dn(0, 1, 1, 0, 1)
            ranks(G - 1)
            sh_at(2, 0)
            for v in range(NS, U0):
                sh_unit(v // NS, v // NS % 2, v % NS)
            sh_end(U0 - 1, FILL, FILL % 2, EXTRA - 1)

            def ex_xt(e, pair, n):
                slot = n // 2
                if n % 2 == 0:
                    pe.wait_ge(in_xe[slot], (pair - slot) * (16 // RX) + 16)
                after(pe, x_lo, e * 2 - 2, 1)
                for c in range(2):
                    last = T.transpose(bank[2 + n % 2][:, c * P:(c + 1) * P], xe[:, n].rearrange("p (d c) -> p c d", c=2)[:, c], ident[:])
                last.then_inc(xt_done, 1)

            def ex_gu(e, n):
                u = n % 2
                pe.wait_ge(x_lo, e * 2 + 2)
                pe.wait_ge(w_lo, e + 1)
                if isinstance(e, int) and e < 2:
                    pe.wait_ge(sa_ready, U0)
                else:
                    pe.wait_ge(a_ready, e - 1)
                for c in range(2):
                    for k, (a, w) in enumerate(PARTS):
                        last = T.matmul(bank[u][:, 0:2 * F].rearrange("p (n f) -> p n f", n=2), xT_parts[a][:, u, c],
                                        gu_parts[w][:, u, :, c], start=(c == 0 and k == 0), stop=(c == 1 and k == 2))
                last.then_inc(gu_done, 1)

            def ex_at(e, n):
                u = n % 2
                pe.wait_ge(a_ready, e + 1)
                if isinstance(e, int) and e < 2:
                    pe.wait_ge(sat_ready, U0)
                else:
                    pe.wait_ge(at_ready, e - 1)
                for c in range(2):
                    last = T.transpose(bank[4 + u][0:HALF, c * P:(c + 1) * P],
                                       act_u[:, u].rearrange("p (f c) -> p c f", c=2)[:, c], ident[:])
                last.then_inc(at_done, 1)

            def ex_dn(e, n):
                u = n % 2
                pe.wait_ge(at_ready, e + 1)
                if isinstance(e, int) and e < 1:
                    pe.wait_ge(sy_read, FILL)
                else:
                    pe.wait_ge(y_ready, e)
                for c in range(2):
                    last = T.matmul(bank[7][:, 0:D], aT[:, u, c], wdn[:, n, c], start=(c == 0), stop=(c == 1))
                last.then_inc(dn_done, 1)

            def ex_step(t, pair, c):
                if not isinstance(t, int) or t + 1 < E:
                    ex_xt(t + 1, pair + (c % 2), (c + 1) % (2 * RX))
                if not isinstance(t, int) or t < E:
                    ex_gu(t, c)
                if not isinstance(t, int) or t >= 2:
                    ex_dn(t - 2, (c - 2) % UN)
                if not isinstance(t, int) or 1 <= t <= E:
                    ex_at(t - 1, (c - 1) % UN)

            ex_xt(0, 0, 0)
            for t in range(FIRST):
                ex_step(t, t // 2, t)
            with pe.Fori(0, (E - UN) // UN) as i:
                for u in range(UN):
                    ex_step(i * UN + (FIRST + u), i * (UN // 2) + (FIRST + u) // 2, (FIRST + u) % UN)
            for t in range(E - UN + FIRST, E):
                ex_step(t, t // 2, t % UN)
            ex_at(E - 1, (E - 1) % UN)
            ex_dn(E - 2, (E - 2) % UN)

            pe.wait_ge(a_ready, E)
            sh_unit(FILL, FILL % 2, EXTRA, 0)
            ex_dn(E - 1, (E - 1) % UN)
            for s in range(EXTRA + 1, NS):
                sh_unit(FILL, FILL % 2, s, 1)
            pe.wait_ge(y_ready, E)
            with pe.Fori(0, (B - FILL - 2) // 2) as i:
                for u in range(2):
                    for s in range(NS):
                        sh_unit(i * 2 + (FILL + 1 + u), (FILL + 1 + u) % 2, s)
            for s in range(NS):
                sh_unit(B - 1, (B - 1) % 2, s)
            sh_end(B * NS - 1, B - 1, (B - 1) % 2, NS - 1)


_INS = ["x", "ctx_2048", "g_xattn", "g_ffn", "L0_xattn_ssm_kernel", "L0_xattn_D", "L0_ffn_w_norm", "L0_ffn_w_router",
        "L0_ffn_w_gate", "L0_ffn_w_up", "L0_ffn_w_down", "L0_ffn_sw_gate", "L0_ffn_sw_up", "L0_ffn_sw_down",
        "L0_ffn_w_shared_gate"]


def kernel(**inputs):
    import numpy as np
    import concourse.bacc as bacc
    from concourse import mybir
    from concourse.bass_utils import run_bass_kernel_spmd as run

    nc = bacc.Bacc("TRN2", target_bir_lowering=False, num_devices=1)
    f32 = mybir.dt.float32
    arrays, args = {}, []
    for name in _INS:
        a = np.ascontiguousarray(inputs[name])
        arrays[f"in_{name}"] = a
        args.append(nc.dram_tensor(f"in_{name}", a.shape, f32, kind="ExternalInput").ap())
    x = inputs["x"]
    heads, taps = inputs["L0_xattn_ssm_kernel"].shape
    experts, width = inputs["L0_ffn_w_gate"].shape[:2]
    out = nc.dram_tensor("out", x.shape, f32, kind="ExternalOutput").ap()
    filt = nc.dram_tensor("filt_scratch", (heads, 128 + taps), f32).ap()
    slots = nc.dram_tensor("slots_scratch", (experts * 128, width), f32).ap()
    yexp = nc.dram_tensor("yexp_scratch", (experts * 128, width), f32).ap()
    build(nc, *args, out, filt, slots, yexp)
    r = run(nc, [arrays], core_ids=[0])
    return r.results[0]["out"]
```
